# Optimizing a Trainium2 kernel written in Bass

```python
import numpy as np
import jax
import jax.numpy as jnp

def _softmax(x, axis=-1):
    return jax.nn.softmax(x, axis=axis)

def _gelu(x):
    return jax.nn.gelu(x, approximate=True)

def _silu(x):
    return jax.nn.silu(x)

def _sigmoid(x):
    return jax.nn.sigmoid(x)

def _layernorm(x, axis=-1, eps=1e-05):
    m = jnp.mean(x, axis=axis, keepdims=True)
    v = jnp.var(x, axis=axis, keepdims=True)
    return (x - m) / jnp.sqrt(v + eps)

def _scatter_add(tgt, idx, src, axis=0):
    return tgt.at[idx].add(src)

def _segment_sum(src, seg, n):
    return jax.ops.segment_sum(src, seg, n)
kernel_name = 'mk_rec_standalone_d1_rec_r8_876dd7'

def setup_inputs(seed: int=0):
    np.random.seed(seed)
    _w = jnp.asarray

    def _rec_inputs():
        import jax
        import jax.numpy as jnp
        _rk = jax.random.key(seed)
        r_A = jax.random.uniform(jax.random.fold_in(_rk, 1), (512, 50, 100), jnp.float32, 0.0, 1)
        r_items = jnp.stack([jax.random.randint(jax.random.fold_in(jax.random.fold_in(_rk, 2), 0), (512,), 5, 99987, jnp.int32), jax.random.randint(jax.random.fold_in(jax.random.fold_in(_rk, 2), 1), (512,), 57, 99995, jnp.int32), jax.random.randint(jax.random.fold_in(jax.random.fold_in(_rk, 2), 2), (512,), 2, 12496, jnp.int32), jax.random.randint(jax.random.fold_in(jax.random.fold_in(_rk, 2), 3), (512,), 33, 99963, jnp.int32), jax.random.randint(jax.random.fold_in(jax.random.fold_in(_rk, 2), 4), (512,), 2, 99964, jnp.int32), jax.random.randint(jax.random.fold_in(jax.random.fold_in(_rk, 2), 5), (512,), 2, 12497, jnp.int32), jax.random.randint(jax.random.fold_in(jax.random.fold_in(_rk, 2), 6), (512,), 43, 12496, jnp.int32), jax.random.randint(jax.random.fold_in(jax.random.fold_in(_rk, 2), 7), (512,), 9, 99981, jnp.int32), jax.random.randint(jax.random.fold_in(jax.random.fold_in(_rk, 2), 8), (512,), 58, 99987, jnp.int32), jax.random.randint(jax.random.fold_in(jax.random.fold_in(_rk, 2), 9), (512,), 10, 99973, jnp.int32), jax.random.randint(jax.random.fold_in(jax.random.fold_in(_rk, 2), 10), (512,), 3, 99983, jnp.int32), jax.random.randint(jax.random.fold_in(jax.random.fold_in(_rk, 2), 11), (512,), 10, 99999, jnp.int32), jax.random.randint(jax.random.fold_in(jax.random.fold_in(_rk, 2), 12), (512,), 15, 99971, jnp.int32), jax.random.randint(jax.random.fold_in(jax.random.fold_in(_rk, 2), 13), (512,), 14, 12497, jnp.int32), jax.random.randint(jax.random.fold_in(jax.random.fold_in(_rk, 2), 14), (512,), 27, 99972, jnp.int32), jax.random.randint(jax.random.fold_in(jax.random.fold_in(_rk, 2), 15), (512,), 0, 99982, jnp.int32), jax.random.randint(jax.random.fold_in(jax.random.fold_in(_rk, 2), 16), (512,), 26, 99995, jnp.int32), jax.random.randint(jax.random.fold_in(jax.random.fold_in(_rk, 2), 17), (512,), 41, 99982, jnp.int32), jax.random.randint(jax.random.fold_in(jax.random.fold_in(_rk, 2), 18), (512,), 6, 99995, jnp.int32), jax.random.randint(jax.random.fold_in(jax.random.fold_in(_rk, 2), 19), (512,), 40, 99908, jnp.int32), jax.random.randint(jax.random.fold_in(jax.random.fold_in(_rk, 2), 20), (512,), 15, 99983, jnp.int32), jax.random.randint(jax.random.fold_in(jax.random.fold_in(_rk, 2), 21), (512,), 5, 99951, jnp.int32), jax.random.randint(jax.random.fold_in(jax.random.fold_in(_rk, 2), 22), (512,), 14, 99970, jnp.int32), jax.random.randint(jax.random.fold_in(jax.random.fold_in(_rk, 2), 23), (512,), 23, 99956, jnp.int32), jax.random.randint(jax.random.fold_in(jax.random.fold_in(_rk, 2), 24), (512,), 97, 99947, jnp.int32), jax.random.randint(jax.random.fold_in(jax.random.fold_in(_rk, 2), 25), (512,), 10, 12498, jnp.int32), jax.random.randint(jax.random.fold_in(jax.random.fold_in(_rk, 2), 26), (512,), 34, 99999, jnp.int32), jax.random.randint(jax.random.fold_in(jax.random.fold_in(_rk, 2), 27), (512,), 15, 99996, jnp.int32), jax.random.randint(jax.random.fold_in(jax.random.fold_in(_rk, 2), 28), (512,), 74, 99898, jnp.int32), jax.random.randint(jax.random.fold_in(jax.random.fold_in(_rk, 2), 29), (512,), 27, 99994, jnp.int32), jax.random.randint(jax.random.fold_in(jax.random.fold_in(_rk, 2), 30), (512,), 38, 99982, jnp.int32), jax.random.randint(jax.random.fold_in(jax.random.fold_in(_rk, 2), 31), (512,), 3, 99946, jnp.int32), jax.random.randint(jax.random.fold_in(jax.random.fold_in(_rk, 2), 32), (512,), 10, 99983, jnp.int32), jax.random.randint(jax.random.fold_in(jax.random.fold_in(_rk, 2), 33), (512,), 7, 99985, jnp.int32), jax.random.randint(jax.random.fold_in(jax.random.fold_in(_rk, 2), 34), (512,), 54, 99973, jnp.int32), jax.random.randint(jax.random.fold_in(jax.random.fold_in(_rk, 2), 35), (512,), 2, 99989, jnp.int32), jax.random.randint(jax.random.fold_in(jax.random.fold_in(_rk, 2), 36), (512,), 1, 99980, jnp.int32), jax.random.randint(jax.random.fold_in(jax.random.fold_in(_rk, 2), 37), (512,), 12, 99964, jnp.int32), jax.random.randint(jax.random.fold_in(jax.random.fold_in(_rk, 2), 38), (512,), 37, 99999, jnp.int32), jax.random.randint(jax.random.fold_in(jax.random.fold_in(_rk, 2), 39), (512,), 23, 99988, jnp.int32), jax.random.randint(jax.random.fold_in(jax.random.fold_in(_rk, 2), 40), (512,), 1, 12496, jnp.int32), jax.random.randint(jax.random.fold_in(jax.random.fold_in(_rk, 2), 41), (512,), 42, 99969, jnp.int32), jax.random.randint(jax.random.fold_in(jax.random.fold_in(_rk, 2), 42), (512,), 37, 99997, jnp.int32), jax.random.randint(jax.random.fold_in(jax.random.fold_in(_rk, 2), 43), (512,), 18, 99979, jnp.int32), jax.random.randint(jax.random.fold_in(jax.random.fold_in(_rk, 2), 44), (512,), 50, 99933, jnp.int32), jax.random.randint(jax.random.fold_in(jax.random.fold_in(_rk, 2), 45), (512,), 19, 12498, jnp.int32), jax.random.randint(jax.random.fold_in(jax.random.fold_in(_rk, 2), 46), (512,), 0, 99994, jnp.int32), jax.random.randint(jax.random.fold_in(jax.random.fold_in(_rk, 2), 47), (512,), 76, 99953, jnp.int32), jax.random.randint(jax.random.fold_in(jax.random.fold_in(_rk, 2), 48), (512,), 14, 99981, jnp.int32), jax.random.randint(jax.random.fold_in(jax.random.fold_in(_rk, 2), 49), (512,), 27, 99945, jnp.int32)], axis=1)
        return (r_A, r_items)
    r_A, r_items = _rec_inputs()

    def _L0_rec_setup():
        import jax, jax.numpy as jnp
        import numpy as np
        B, N, H, V = (512, 50, 128, 12500)
        STEP = 1

        def _gnn_cell(A, hidden, w_in, b_in, w_out, b_out, w_ih, w_hh, b_ih, b_hh, b_iah, b_oah):
            n = A.shape[1]
            input_in = jnp.matmul(A[:, :, :n], hidden @ w_in.T + b_in) + b_iah
            input_out = jnp.matmul(A[:, :, n:], hidden @ w_out.T + b_out) + b_oah
            inputs = jnp.concatenate([input_in, input_out], axis=2)
            gi = inputs @ w_ih.T + b_ih
            gh = hidden @ w_hh.T + b_hh
            i_r, i_i, i_n = jnp.split(gi, 3, axis=2)
            h_r, h_i, h_n = jnp.split(gh, 3, axis=2)
            resetgate = jax.nn.sigmoid(i_r + h_r)
            inputgate = jax.nn.sigmoid(i_i + h_i)
            newgate = jnp.tanh(i_n + resetgate * h_n)
            return newgate + inputgate * (hidden - newgate)
        key = jax.random.key(seed)
        ks = jax.random.split(key, 14)
        stdv = 1.0 / np.sqrt(H)

        def u(k, shape):
            return jax.random.uniform(k, shape, jnp.float32, -stdv, stdv)
        items = jax.random.randint(ks[0], (B, N), 0, V + 1)
        A = jax.random.uniform(ks[1], (B, N, 2 * N), jnp.float32)
        return {'items': items, 'A': A, 'emb': u(ks[2], (V + 1, H)), 'w_in': u(ks[3], (H, H)), 'b_in': u(ks[4], (H,)), 'w_out': u(ks[5], (H, H)), 'b_out': u(ks[6], (H,)), 'w_ih': u(ks[7], (3 * H, 2 * H)), 'w_hh': u(ks[8], (3 * H, H)), 'b_ih': u(ks[9], (3 * H,)), 'b_hh': u(ks[10], (3 * H,)), 'b_iah': u(ks[11], (H,)), 'b_oah': u(ks[12], (H,))}
    _L0_rec_all = _L0_rec_setup()
    _L0_rec_in = {k: v for k, v in _L0_rec_all.items() if k in ('emb', 'w_in', 'b_in', 'w_out', 'b_out', 'w_ih', 'w_hh', 'b_ih', 'b_hh', 'b_iah', 'b_oah')}
    del _L0_rec_all
    return {'r_A': r_A, 'r_items': r_items, 'L0_rec_emb': _L0_rec_in['emb'], 'L0_rec_w_in': _L0_rec_in['w_in'], 'L0_rec_b_in': _L0_rec_in['b_in'], 'L0_rec_w_out': _L0_rec_in['w_out'], 'L0_rec_b_out': _L0_rec_in['b_out'], 'L0_rec_w_ih': _L0_rec_in['w_ih'], 'L0_rec_w_hh': _L0_rec_in['w_hh'], 'L0_rec_b_ih': _L0_rec_in['b_ih'], 'L0_rec_b_hh': _L0_rec_in['b_hh'], 'L0_rec_b_iah': _L0_rec_in['b_iah'], 'L0_rec_b_oah': _L0_rec_in['b_oah']}

def reference(r_A, r_items, L0_rec_emb, L0_rec_w_in, L0_rec_b_in, L0_rec_w_out, L0_rec_b_out, L0_rec_w_ih, L0_rec_w_hh, L0_rec_b_ih, L0_rec_b_hh, L0_rec_b_iah, L0_rec_b_oah):
    import jax
    import jax.numpy as jnp

    def _L0_rec_ref(items, A, emb, w_in, b_in, w_out, b_out, w_ih, w_hh, b_ih, b_hh, b_iah, b_oah):
        import jax, jax.numpy as jnp
        import numpy as np
        B, N, H, V = (512, 50, 128, 12500)
        STEP = 1

        def _gnn_cell(A, hidden, w_in, b_in, w_out, b_out, w_ih, w_hh, b_ih, b_hh, b_iah, b_oah):
            n = A.shape[1]
            input_in = jnp.matmul(A[:, :, :n], hidden @ w_in.T + b_in) + b_iah
            input_out = jnp.matmul(A[:, :, n:], hidden @ w_out.T + b_out) + b_oah
            inputs = jnp.concatenate([input_in, input_out], axis=2)
            gi = inputs @ w_ih.T + b_ih
            gh = hidden @ w_hh.T + b_hh
            i_r, i_i, i_n = jnp.split(gi, 3, axis=2)
            h_r, h_i, h_n = jnp.split(gh, 3, axis=2)
            resetgate = jax.nn.sigmoid(i_r + h_r)
            inputgate = jax.nn.sigmoid(i_i + h_i)
            newgate = jnp.tanh(i_n + resetgate * h_n)
            return newgate + inputgate * (hidden - newgate)
        hidden = emb[items]
        for _ in range(STEP):
            hidden = _gnn_cell(A, hidden, w_in, b_in, w_out, b_out, w_ih, w_hh, b_ih, b_hh, b_iah, b_oah)
        return hidden
    y = _L0_rec_ref(r_items, r_A, L0_rec_emb, L0_rec_w_in, L0_rec_b_in, L0_rec_w_out, L0_rec_b_out, L0_rec_w_ih, L0_rec_w_hh, L0_rec_b_ih, L0_rec_b_hh, L0_rec_b_iah, L0_rec_b_oah)
    return y

_drawn_inputs = setup_inputs


def setup_inputs(seed=0):
    import zlib

    import numpy as np

    out = dict(_drawn_inputs(seed))
    spreads = {}
    factors = {'L0_rec_w_hh': 2.912}
    for name, (base, spread) in spreads.items():
        noise = np.random.default_rng([zlib.crc32(name.encode()), seed]).standard_normal(out[name].shape)
        drawn = base * np.exp(spread * noise) if base else spread * noise
        out[name] = jnp.asarray(drawn.astype(out[name].dtype))
    for name, factor in factors.items():
        out[name] = (out[name] * factor).astype(out[name].dtype)
    return out
```

```python
import concourse.bass as bass
from concourse import mybir
from contextlib import ExitStack


def gnn_cell_kernel(nc, A, items, emb, w_in, b_in, w_out, b_out, w_ih, w_hh, b_ih, b_hh, b_iah, b_oah, out):
    fp32 = mybir.dt.float32
    fp32r = mybir.dt.float32r
    i32 = mybir.dt.int32
    u32 = mybir.dt.uint32
    ALU = mybir.AluOpType
    ACT = mybir.ActivationFunctionType
    AX = mybir.AxisListType

    B, N = items.shape
    V, H = emb.shape
    CB = 8
    CT = CB * N
    NCH = B // CB
    CTILES = CB // 2
    HALF = 64
    PAD = HALF - N
    P2 = 2 * N
    G = 3
    SKIP = float(1 << 20)
    BANK = 512
    RS = 3

    A_rows = A.rearrange("(c g q) i (d j) -> d c (q i) g j", g=CTILES, q=2, d=2)
    out_rows = out.rearrange("(c g q) i f -> c (q i) g f", g=CTILES, q=2)
    items_rows = items.rearrange("(Q s q) i -> s Q q i", s=2, q=2)

    ctx = ExitStack()
    with ctx:
        def sb(name, shape, dt=fp32):
            return ctx.enter_context(nc.sbuf_tensor(name, shape, dt))

        def bank(name):
            return ctx.enter_context(nc.psum_tensor(name, [128, BANK], fp32))

        def sem(name):
            return ctx.enter_context(nc.semaphore(name))

        def pair(name, shape, dt=fp32):
            return [sb(f"{name}{i}", shape, dt) for i in range(2)]

        ident = sb("ident", [128, 128])
        w_in_sb = sb("w_in_sb", [128, H])
        w_out_sb = sb("w_out_sb", [128, H])
        w_ih_sb = sb("w_ih_sb", [128, G, 2 * H])
        w_hh_sb = sb("w_hh_sb", [128, G, H])
        b_sb = sb("b_sb", [128, 4])
        bg_sb = sb("bg_sb", [128, 2, G])
        w_ihT = sb("w_ihT", [128, 2, G * H])
        b_rows = sb("b_rows", [128, 2, 128])
        hi_rows = sb("hi_rows", [128, 1])
        lo_rows = sb("lo_rows", [128, 1])
        C_hi = sb("C_hi", [128, 3, G * H], fp32r)
        C_lo = sb("C_lo", [128, 3, G * H], fp32r)
        v_hi = sb("v_hi", [128, G * H], fp32r)
        v_lo = sb("v_lo", [128, G * H])
        v_mask = sb("v_mask", [128, G * H])
        v_rows = sb("v_rows", [128, G * H], fp32r)
        gate_bias = sb("gate_bias", [128, G])
        items_sb = sb("items_sb", [128, 2, 2, N], i32)
        items_f = sb("items_f", [128, 2, 2, HALF])
        items_neg = sb("items_neg", [128, 2, 2, HALF])
        idx_all = sb("idx_all", [128, B // 2 + CTILES], u32)

        idx = pair("idx", [128, CTILES], u32)
        A_nat = pair("A_nat", [128, 2, CTILES, HALF])
        rs = pair("rs", [128, 2, CTILES])
        h_nat = pair("h_nat", [128, CTILES, H])
        A_bd = sb("A_bd", [128, 2, 2, 2, P2])
        rs_bd = pair("rs_bd", [128, 2, 2, P2], fp32r)
        hT = pair("hT", [128, CT])
        hT_hi = pair("hT_hi", [128, CT], fp32r)
        hT_lo = pair("hT_lo", [128, CT], fp32r)
        u_hi = pair("u_hi", [128, 2, CT], fp32r)
        u_lo = pair("u_lo", [128, 2, CT], fp32r)
        r_sb = pair("r_sb", [128, CT])
        z_sb = pair("z_sb", [128, CT])
        n_sb = pair("n_sb", [128, CT])
        t_sb = pair("t_sb", [128, CT])
        p_sb = pair("p_sb", [128, CT])
        d_sb = pair("d_sb", [128, CT])
        e_sb = pair("e_sb", [128, CT])
        o_sb = pair("o_sb", [128, CT])
        out_sb = pair("out_sb", [128, CTILES, H])

        ps_x = bank("ps_x")
        ps_h = bank("ps_h")
        ps_u = ctx.enter_context(nc.psum_tensor("ps_u", [128, 2, BANK], fp32))
        ps_r = bank("ps_r")
        ps_z = bank("ps_z")
        ps_in = bank("ps_in")
        ps_hn = bank("ps_hn")

        zeroed = sem("zeroed")
        ident_made = sem("ident_made")
        weights_in = sem("weights_in")
        biases_in = sem("biases_in")
        items_in = sem("items_in")
        s_idx = sem("s_idx")
        s_idxT = sem("s_idxT")
        idx_made = sem("idx_made")
        s_wT = sem("s_wT")
        s_wTe = sem("s_wTe")
        s_C = sem("s_C")
        s_Ce = sem("s_Ce")
        s_brows = sem("s_brows")
        s_vc = sem("s_vc")
        s_v = sem("s_v")
        setup_done = sem("setup_done")

        A_loaded = [sem(f"A_loaded{i}") for i in range(2)]
        h_loaded = [sem(f"h_loaded{i}") for i in range(2)]
        out_stored = [sem(f"out_stored{i}") for i in range(2)]
        idx_staged = sem("idx_staged")
        rs_summed = sem("rs_summed")
        rs_hi_put = sem("rs_hi_put")
        rs_put = sem("rs_put")
        AT_done = sem("AT_done")
        hT_done = sem("hT_done")
        agg_done = sem("agg_done")
        hn_done = sem("hn_done")
        r_done = sem("r_done")
        z_done = sem("z_done")
        in_done = sem("in_done")
        outT_done = sem("outT_done")
        A_placed = sem("A_placed")
        hT_copied = sem("hT_copied")
        hT_hi_made = sem("hT_hi_made")
        hT_lo_made = sem("hT_lo_made")
        u_hi_made = sem("u_hi_made")
        u_lo_made = sem("u_lo_made")
        r_made = sem("r_made")
        z_made = sem("z_made")
        n_made = sem("n_made")
        t_made = sem("t_made")
        p_made = sem("p_made")
        d_made = sem("d_made")
        e_made = sem("e_made")
        o_made = sem("o_made")
        out_copied = sem("out_copied")

        def chunks(eng, step):
            for par in range(2):
                step(par, 0, par)
            with eng.Fori(1, NCH // 2 - 1) as k:
                for par in range(2):
                    step(2 * k + par, k, par)
            for par in range(2):
                step(NCH - 2 + par, NCH // 2 - 1, par)

        def number(c):
            return isinstance(c, int)

        block = ctx.enter_context(nc.Block())

        @block.sync
        def _(sp):
            for s in range(2):
                for half in range(2):
                    sp.dma_start(items_sb[:, half, s, :],
                                 items_rows[s, half * 64:half * 64 + 64, :, :]).then_inc(items_in, 16)
            sp.dma_start(w_ih_sb[:, :, :], w_ih.rearrange("(g p) k -> p g k", p=128)).then_inc(weights_in, 16)
            sp.dma_start(w_hh_sb[:, :, :], w_hh.rearrange("(g p) k -> p g k", p=128)).then_inc(weights_in, 16)
            sp.dma_start(w_in_sb[:, :], w_in).then_inc(weights_in, 16)
            sp.dma_start(w_out_sb[:, :], w_out).then_inc(weights_in, 16)

            def load_A(c, par):
                for d in range(2):
                    sp.dma_start(A_nat[par][0:P2, d, :, PAD:HALF],
                                 A_rows[d, bass.ds(c, 1), :, :, :].rearrange("c p g j -> (c p) g j"))\
                      .then_inc(A_loaded[par], 16)

            sp.wait_ge(zeroed, 1)
            load_A(0, 0)
            load_A(1, 1)

            def store(c, par):
                sp.wait_ge(out_copied, c + 1)
                sp.dma_start(out_rows[bass.ds(c, 1), :, :, :].rearrange("c p g f -> (c p) g f"),
                             out_sb[par][0:P2, :, :]).then_inc(out_stored[par], 16)

            def step(c, k, par):
                if not (number(c) and c + 2 >= NCH):
                    sp.wait_ge(AT_done, c + 1)
                    load_A(c + 2, par)
                if not (number(c) and c < 2):
                    store(c - 2, par)

            chunks(sp, step)
            for par in range(2):
                store(NCH - 2 + par, par)
            for par in range(2):
                sp.wait_ge(out_stored[par], 16 * (NCH // 2))

        @block.gpsimd
        def _(pool):
            pool.memset(ident[:, :], 0.0).then_inc(ident_made, 1)
            pool.wait_ge(ident_made, 1)
            pool.affine_select(out=ident[:, :], in_=ident[:, :], compare_op=ALU.not_equal, fill=1.0,
                               base=0, pattern=[[-1, 128]], channel_multiplier=1).then_inc(ident_made, 1)
            pool.memset(lo_rows[:, :], 0.0).then_inc(s_brows, 1)
            for n, row in enumerate([1, 1 + RS, HALF + 1, HALF + 1 + RS]):
                pool.wait_ge(s_brows, n + 1)
                pool.affine_select(out=lo_rows[:, :], in_=lo_rows[:, :], compare_op=ALU.not_equal, fill=1.0,
                                   base=-row, pattern=[[0, 1]], channel_multiplier=1).then_inc(s_brows, 1)
            pool.wait_ge(idx_made, 2)

            def stage_indices(c, par):
                pool.tensor_copy(idx[par][:, :], idx_all[:, bass.ds(c * CTILES, CTILES)]).then_inc(idx_staged, 1)

            def gather(par):
                for t in range(CTILES):
                    pool.indirect_dma_start(
                        out=h_nat[par][:, t, :], out_offset=None, in_=emb,
                        in_offset=bass.IndirectOffsetOnAxis(ap=idx[par][:, t:t + 1], axis=0),
                        bounds_check=V - 1, oob_is_err=False).then_inc(h_loaded[par], 16)

            stage_indices(0, 0)
            stage_indices(1, 1)
            pool.wait_ge(idx_staged, 2)
            pool.wait_ge(zeroed, 1)
            gather(0)
            gather(1)
            pool.wait_ge(h_loaded[0], 16 * CTILES)
            stage_indices(2, 0)

            def step(c, k, par):
                if not (number(c) and c + 2 >= NCH):
                    pool.wait_ge(agg_done, c + 1)
                    pool.wait_ge(idx_staged, c + 3)
                    if not (number(c) and c + 3 >= NCH):
                        pool.wait_ge(h_loaded[1 - par], 16 * CTILES * (k + par + 1))
                        stage_indices(c + 3, 1 - par)
                    gather(par)

            chunks(pool, step)

        @block.scalar
        def _(act):
            for n, b in enumerate((b_in, b_out, b_iah, b_oah)):
                act.dma_start(b_sb[:, n:n + 1], b.rearrange("(p o) -> p o", o=1)).then_inc(biases_in, 16)
            for n, b in enumerate((b_ih, b_hh)):
                for g in range(G):
                    act.dma_start(bg_sb[:, n, g:g + 1],
                                  b[g * 128:g * 128 + 128].rearrange("(p o) -> p o", o=1)).then_inc(biases_in, 16)
            act.wait_ge(s_wT, 1)
            act.activation(w_ihT[:, 0, :], ps_r[:, 0:G * H], ACT.Copy)
            act.activation(w_ihT[:, 1, :], ps_z[:, 0:G * H], ACT.Copy).then_inc(s_wTe, 1)
            act.activation(C_hi[:, 2, :], ps_hn[:, 0:G * H], ACT.Copy).then_inc(s_Ce, 1)
            act.wait_ge(s_C, 1)
            act.activation(C_hi[:, 0, :], ps_u[:, 0, 0:G * H], ACT.Copy)
            act.activation(C_hi[:, 1, :], ps_u[:, 1, 0:G * H], ACT.Copy)
            act.activation(v_hi[:, :], ps_in[:, 0:G * H], ACT.Copy).then_inc(s_Ce, 1)

            def prepare(c, par):
                act.wait_ge(AT_done, c + 1)
                if not (number(c) and c < 1):
                    act.wait_ge(agg_done, c)
                if not (number(c) and c < 2):
                    act.wait_ge(in_done, c - 1)
                x = ps_x[:, 0:2 * 2 * P2].rearrange("p (Q d t) -> p Q d t", Q=2, d=2)
                for s in range(2):
                    lo = s * HALF
                    act.activation(A_bd[lo:lo + HALF, :, s, :, :], x[lo:lo + HALF, :, :, :], ACT.Copy)
                    last = act.activation(rs_bd[par][lo:lo + 32, :, s, :], x[lo:lo + 32, :, 0, :], ACT.Copy)
                last.then_inc(A_placed, 1)
                act.wait_ge(hT_done, c + 1)
                if not (number(c) and c < 2):
                    act.wait_ge(d_made, c - 1)
                src = ps_h[:, :].rearrange("p (Q q s i) -> p Q q s i", Q=2, q=2, s=2)
                dst = hT[par][:, :].rearrange("p (Q s q i) -> p Q q s i", Q=2, s=2, q=2)
                for Q in range(2):
                    last = act.activation(dst[:, Q], src[:, Q, :, :, PAD:HALF], ACT.Copy)
                last.then_inc(hT_copied, 1)

            def split_u(c, par):
                act.wait_ge(agg_done, c + 1)
                if not (number(c) and c < 2):
                    act.wait_ge(in_done, c - 1)
                src = ps_u[:, :, 0:CT].rearrange("p Q (d t) -> p Q d t", d=2)
                dst = u_hi[par][:, :, :].rearrange("p d (Q t) -> p Q d t", Q=2)
                act.activation(dst, src, ACT.Copy).then_inc(u_hi_made, 1)

            def copy_out(c, k, par):
                act.wait_ge(outT_done, c + 1)
                if not (number(k) and k < 1):
                    act.wait_ge(out_stored[par], 16 * k)
                act.activation(out_sb[par][0:P2, :, :],
                               ps_x[0:P2, :].rearrange("p (g f) -> p g f", g=CTILES), ACT.Copy)\
                   .then_inc(out_copied, 1)

            act.wait_ge(zeroed, 1)
            prepare(0, 0)
            split_u(0, 0)
            act.wait_ge(setup_done, 1)

            def step(c, k, par):
                if not (number(c) and c + 1 >= NCH):
                    prepare(c + 1, 1 - par)
                act.wait_ge(r_done, c + 1)
                if not (number(c) and c < 2):
                    act.wait_ge(t_made, c - 1)
                act.activation(r_sb[par][:, :], ps_r[:, 0:CT], ACT.Sigmoid, bias=gate_bias[:, 0:1]).then_inc(r_made, 1)
                if not (number(c) and c + 1 >= NCH):
                    split_u(c + 1, 1 - par)
                act.wait_ge(z_done, c + 1)
                if not (number(c) and c < 2):
                    act.wait_ge(e_made, c - 1)
                act.activation(z_sb[par][:, :], ps_z[:, 0:CT], ACT.Sigmoid, bias=gate_bias[:, 1:2]).then_inc(z_made, 1)
                if not (number(c) and c < 1):
                    copy_out(c - 1, k if par else k - 1, 1 - par)
                act.wait_ge(p_made, c + 1)
                if not (number(c) and c < 2):
                    act.wait_ge(o_made, c - 1)
                act.activation(n_sb[par][:, :], p_sb[par][:, :], ACT.Tanh, bias=gate_bias[:, 2:3]).then_inc(n_made, 1)

            chunks(act, step)
            copy_out(NCH - 1, NCH // 2 - 1, 1)

        @block.vector
        def _(dve):
            for t in (A_nat[0], A_nat[1], h_nat[0], h_nat[1], A_bd):
                dve.memset(t[:], 0.0)
            for t in rs_bd:
                dve.memset(t[:].bitcast(fp32), 0.0)
            dve.memset(b_rows[:], 0.0)
            dve.memset(idx_all[:, B // 2:B // 2 + CTILES], 0)
            dve.memset(items_f[:], SKIP).then_inc(zeroed, 1)

            dve.wait_ge(zeroed, 1)
            dve.wait_ge(items_in, 64)
            body = items_f[:, :, :, PAD:HALF]
            neg = items_neg[:, :, :, PAD:HALF]
            dve.tensor_copy(body, items_sb[:, :, :, :]).then_inc(s_idx, 1)
            dve.wait_ge(s_idx, 1)
            dve.tensor_scalar(neg, body, 0.0, float(V), ALU.is_lt, ALU.mult).then_inc(s_idx, 1)
            dve.wait_ge(s_idx, 2)
            dve.tensor_tensor(body, body, neg, ALU.add).then_inc(s_idx, 1)
            dve.wait_ge(s_idx, 3)
            dve.tensor_scalar(body, body, 0.0, float(V - 1), ALU.max, ALU.min).then_inc(s_idx, 1)
            dve.wait_ge(s_idxT, 1)
            for half in range(2):
                dve.tensor_copy(idx_all[:, half * 128:half * 128 + 128],
                                ps_h[:, half * 128:half * 128 + 128]).then_inc(idx_made, 1)

            dve.wait_ge(biases_in, 160)
            for half in range(2):
                for d in range(2):
                    at = half * HALF + d * RS
                    last = dve.tensor_copy(b_rows[:, d, at:at + RS], b_sb[:, d:d + 1].to_broadcast([128, RS]))
            last.then_inc(s_vc, 1)
            dve.wait_ge(s_brows, 5)
            dve.tensor_scalar(hi_rows[:, :], lo_rows[:, :], -1.0, 1.0, ALU.mult, ALU.add).then_inc(s_v, 1)
            dve.wait_ge(s_Ce, 1)
            dve.tensor_tensor(C_lo[:, 2, :], ps_hn[:, 0:G * H], C_hi[:, 2, :].bitcast(fp32), ALU.subtract)
            dve.wait_ge(s_Ce, 2)
            for d in range(2):
                dve.tensor_tensor(C_lo[:, d, :], ps_u[:, d, 0:G * H], C_hi[:, d, :].bitcast(fp32), ALU.subtract)
            dve.tensor_tensor(v_lo[:, :], ps_in[:, 0:G * H], v_hi[:, :].bitcast(fp32), ALU.subtract).then_inc(s_v, 1)
            dve.wait_ge(s_v, 2)
            dve.tensor_scalar(v_mask[:, :], v_lo[:, :], lo_rows[:, 0:1], None, ALU.mult).then_inc(s_v, 1)
            dve.wait_ge(s_v, 3)
            dve.scalar_tensor_tensor(out=v_rows[:, :], in0=v_hi[:, :].bitcast(fp32), scalar=hi_rows[:, 0:1],
                                     in1=v_mask[:, :], op0=ALU.mult, op1=ALU.add)
            dve.tensor_tensor(gate_bias[:, :], ps_r[:, BANK - G:BANK], bg_sb[:, 0, :], ALU.add).then_inc(s_v, 1)
            dve.wait_ge(s_v, 4)
            dve.tensor_tensor(gate_bias[:, 0:2], gate_bias[:, 0:2], bg_sb[:, 1, 0:2], ALU.add).then_inc(setup_done, 1)

            def put_row_sums(c, k, par):
                dve.wait_ge(A_loaded[par], 32 * (k + 1))
                dve.tensor_reduce(out=rs[par][0:P2, :, :],
                                  in_=A_nat[par][0:P2, :, :, PAD:HALF],
                                  axis=AX.X, op=ALU.add).then_inc(rs_summed, 1)
                dve.wait_ge(rs_summed, c + 1)
                slots = A_nat[par][0:P2, 0, :, 0:2 * RS].rearrange("p g (d x) -> p d g x", d=2)
                dve.tensor_copy(slots[:, :, :, 0:2].bitcast(fp32r),
                                rs[par][0:P2, :, :].unsqueeze(3).to_broadcast([P2, 2, CTILES, 2]))\
                   .then_inc(rs_hi_put, 1)
                dve.wait_ge(rs_hi_put, c + 1)
                dve.tensor_tensor(slots[:, :, :, 2], rs[par][0:P2, :, :], slots[:, :, :, 0], ALU.subtract)\
                   .then_inc(rs_put, 1)

            def split_h(c, par):
                dve.wait_ge(hT_copied, c + 1)
                if not (number(c) and c < 2):
                    dve.wait_ge(z_done, c - 1)
                dve.tensor_copy(hT_hi[par][:, :], hT[par][:, :]).then_inc(hT_hi_made, 1)
                dve.wait_ge(hT_hi_made, c + 1)
                dve.tensor_tensor(hT_lo[par][:, :], hT[par][:, :], hT_hi[par][:, :].bitcast(fp32), ALU.subtract)\
                   .then_inc(hT_lo_made, 1)

            def split_u(c, par):
                dve.wait_ge(u_hi_made, c + 1)
                src = ps_u[:, :, 0:CT].rearrange("p Q (d t) -> p Q d t", d=2)
                hi = u_hi[par][:, :, :].rearrange("p d (Q t) -> p Q d t", Q=2).bitcast(fp32)
                dst = u_lo[par][:, :, :].rearrange("p d (Q t) -> p Q d t", Q=2)
                dve.tensor_tensor(dst, src, hi, ALU.subtract).then_inc(u_lo_made, 1)

            put_row_sums(0, 0, 0)
            split_h(0, 0)
            split_u(0, 0)
            put_row_sums(1, 0, 1)

            def step(c, k, par):
                if not (number(c) and c + 1 >= NCH):
                    split_h(c + 1, 1 - par)
                dve.wait_ge(r_made, c + 1)
                dve.wait_ge(hn_done, c + 1)
                dve.scalar_tensor_tensor(out=t_sb[par][:, :], in0=ps_hn[:, 0:CT], scalar=bg_sb[:, 1, 2:3],
                                         in1=r_sb[par][:, :], op0=ALU.add, op1=ALU.mult).then_inc(t_made, 1)
                if not (number(c) and c + 1 >= NCH):
                    split_u(c + 1, 1 - par)
                if not (number(c) and c + 2 >= NCH):
                    put_row_sums(c + 2, k + 1, par)
                dve.wait_ge(in_done, c + 1)
                dve.wait_ge(t_made, c + 1)
                dve.tensor_tensor(p_sb[par][:, :], ps_in[:, 0:CT], t_sb[par][:, :], ALU.add).then_inc(p_made, 1)
                dve.wait_ge(n_made, c + 1)
                dve.tensor_tensor(d_sb[par][:, :], hT[par][:, :], n_sb[par][:, :], ALU.subtract).then_inc(d_made, 1)
                dve.wait_ge(d_made, c + 1)
                dve.wait_ge(z_made, c + 1)
                dve.tensor_tensor(e_sb[par][:, :], d_sb[par][:, :], z_sb[par][:, :], ALU.mult).then_inc(e_made, 1)
                dve.wait_ge(e_made, c + 1)
                if not (number(c) and c < 2):
                    dve.wait_ge(outT_done, c - 1)
                dve.tensor_tensor(o_sb[par][:, :], e_sb[par][:, :], n_sb[par][:, :], ALU.add).then_inc(o_made, 1)

            chunks(dve, step)

        @block.tensor
        def _(pe):
            pe.wait_ge(ident_made, 2)
            pe.wait_ge(s_idx, 4)
            for half in range(2):
                last = pe.transpose(ps_h[:, half * 128:half * 128 + 128],
                                    items_f[:, half, :, :].rearrange("p s i -> p (s i)"), ident[:, :])
            last.then_inc(s_idxT, 1)
            pe.wait_ge(weights_in, 64)
            for g in range(G):
                at = slice(g * H, g * H + H)
                pe.transpose(ps_r[:, at], w_ih_sb[:, g, 0:H], ident[:, :])
                pe.transpose(ps_z[:, at], w_ih_sb[:, g, H:2 * H], ident[:, :])
                last = pe.transpose(ps_hn[:, at], w_hh_sb[:, g, :], ident[:, :])
            last.then_inc(s_wT, 1)
            pe.wait_ge(s_wTe, 1)
            pe.wait_ge(s_vc, 1)
            pe.matmul(ps_u[:, 0, 0:G * H], w_in_sb[:, :], w_ihT[:, 0, :], start=True, stop=True)
            pe.matmul(ps_u[:, 1, 0:G * H], w_out_sb[:, :], w_ihT[:, 1, :], start=True, stop=True)
            for d in range(2):
                pe.matmul(ps_in[:, 0:G * H], b_rows[:, d, :], w_ihT[:, d, :], start=d == 0, stop=d == 1)
            for g in range(G):
                for d in range(2):
                    last = pe.matmul(ps_r[:, BANK - G + g:BANK - G + g + 1], w_ihT[:, d, g * H:g * H + H],
                                     b_sb[:, 2 + d:3 + d], start=d == 0, stop=d == 1)
            last.then_inc(s_C, 1)

            def transpose_in(c, k, par):
                pe.wait_ge(A_loaded[par], 32 * (k + 1))
                pe.wait_ge(rs_put, c + 1)
                if not (number(c) and c < 3):
                    pe.wait_ge(out_copied, c - 2)
                for Q in range(2):
                    for d in range(2):
                        at = (2 * Q + d) * P2
                        last = pe.transpose(ps_x[:, at:at + P2],
                                            A_nat[par][0:P2, d, 2 * Q:2 * Q + 2, :].rearrange("p s j -> p (s j)"),
                                            ident[0:P2, 0:P2])
                last.then_inc(AT_done, 1)
                pe.wait_ge(h_loaded[par], 16 * CTILES * (k + 1))
                if not (number(c) and c < 1):
                    pe.wait_ge(hT_copied, c)
                else:
                    pe.wait_ge(idx_made, 2)
                for t in range(CTILES):
                    last = pe.transpose(ps_h[:, t * 128:t * 128 + 128], h_nat[par][:, t, :], ident[:, :])
                last.then_inc(hT_done, 1)

            def aggregate(c, par):
                pe.wait_ge(A_placed, c + 1)
                if not (number(c) and c < 1):
                    pe.wait_ge(u_lo_made, c)
                for Q in range(2):
                    u = ps_u[:, Q, 0:CT].rearrange("p (d s q i) -> p s d q i", d=2, s=2, q=2)
                    for q in range(2):
                        last = pe.matmul(u[:, :, :, q, :], h_nat[par][:, 2 * Q + q, :],
                                         A_bd[:, Q, :, :, q * N:q * N + N], start=True, stop=True)
                last.then_inc(agg_done, 1)

            def gate(psum, g, par, terms):
                at = slice(g * H, g * H + H)
                products = []
                for w, hi, lo in terms:
                    products += [(C_hi[:, w, at], hi), (C_lo[:, w, at], hi), (C_hi[:, w, at], lo)]
                if terms[0][0] == 0:
                    products.append((v_rows[:, at], rs_bd[par][:, :, :, :].rearrange("p Q s t -> p (Q s t)")))
                for n, (w, x) in enumerate(products):
                    last = pe.matmul(psum[:, 0:CT], w, x, start=n == 0, stop=n == len(products) - 1)
                return last

            transpose_in(0, 0, 0)
            pe.wait_ge(setup_done, 1)
            aggregate(0, 0)

            def step(c, k, par):
                of_u = [(d, u_hi[par][:, d, :], u_lo[par][:, d, :]) for d in range(2)]
                of_h = [(2, hT_hi[par][:, :], hT_lo[par][:, :])]
                more = not (number(c) and c + 1 >= NCH)
                if more:
                    transpose_in(c + 1, k + par, 1 - par)
                pe.wait_ge(hT_lo_made, c + 1)
                if not (number(c) and c < 1):
                    pe.wait_ge(t_made, c)
                gate(ps_hn, 2, par, of_h).then_inc(hn_done, 1)
                pe.wait_ge(u_lo_made, c + 1)
                if not (number(c) and c < 1):
                    pe.wait_ge(r_made, c)
                gate(ps_r, 0, par, of_u + of_h).then_inc(r_done, 1)
                if more:
                    aggregate(c + 1, 1 - par)
                if not (number(c) and c < 1):
                    pe.wait_ge(z_made, c)
                gate(ps_z, 1, par, of_u + of_h).then_inc(z_done, 1)
                if not (number(c) and c < 1):
                    transpose_out(c - 1, 1 - par, more)
                if not (number(c) and c < 1):
                    pe.wait_ge(p_made, c)
                gate(ps_in, 2, par, of_u).then_inc(in_done, 1)

            def transpose_out(c, par, more):
                pe.wait_ge(o_made, c + 1)
                if more:
                    pe.wait_ge(A_placed, c + 3)
                else:
                    pe.wait_ge(out_copied, c)
                for t in range(CTILES):
                    last = pe.transpose(ps_x[0:P2, t * H:t * H + H], o_sb[par][:, t * P2:t * P2 + P2], ident[:, :])
                last.then_inc(outT_done, 1)

            chunks(pe, step)
            transpose_out(NCH - 1, 1, False)


_INS = ['r_A', 'r_items', 'L0_rec_emb', 'L0_rec_w_in', 'L0_rec_b_in', 'L0_rec_w_out', 'L0_rec_b_out',
        'L0_rec_w_ih', 'L0_rec_w_hh', 'L0_rec_b_ih', 'L0_rec_b_hh', 'L0_rec_b_iah', 'L0_rec_b_oah']


def kernel(**inputs):
    import numpy as _np
    import concourse.bacc as _bacc
    from concourse import mybir as _mybir
    from concourse.bass_utils import run_bass_kernel_spmd as _run

    nc = _bacc.Bacc("TRN2", target_bir_lowering=False, num_devices=1)
    arrays, args = {}, []
    for name in _INS:
        a = _np.ascontiguousarray(inputs[name])
        arrays[f"in_{name}_dram"] = a
        args.append(nc.dram_tensor(f"in_{name}_dram", a.shape, _mybir.dt.from_np(a.dtype), kind="ExternalInput").ap())
    B, N = arrays["in_r_items_dram"].shape
    H = arrays["in_L0_rec_emb_dram"].shape[1]
    args.append(nc.dram_tensor("out_0_dram", (B, N, H), _mybir.dt.float32, kind="ExternalOutput").ap())
    gnn_cell_kernel(nc, *args)
    r = _run(nc, [arrays], core_ids=[0])
    return r.results[0]["out_0_dram"]
```

```python
import concourse.bass as bass
from concourse import mybir
from contextlib import ExitStack


def gnn_cell_kernel(nc, A, items, emb, w_in, b_in, w_out, b_out, w_ih, w_hh, b_ih, b_hh, b_iah, b_oah, out):
    fp32 = mybir.dt.float32
    fp32r = mybir.dt.float32r
    i32 = mybir.dt.int32
    u32 = mybir.dt.uint32
    ALU = mybir.AluOpType
    ACT = mybir.ActivationFunctionType
    AX = mybir.AxisListType

    B, N = items.shape
    V, H = emb.shape
    CB = 8
    CT = CB * N
    NCH = B // CB
    CTILES = CB // 2
    HALF = 64
    ROWS = HALF + N
    P2 = 2 * N
    G = 3
    SKIP = float(1 << 20)
    BANK = 512
    RS = 3

    A_rows = A.rearrange("(c g q) i (d j) -> d c (q i) g j", g=CTILES, q=2, d=2)
    FULL = [CT // 128, (2 * CT - CT // 128 * 128) // 128]
    FROM = [0, FULL[0] * 128]
    REST = 2 * CT - (FULL[0] + FULL[1]) * 128
    REST_AT = 2 * CT - REST
    out_pairs = out.rearrange("(k b) i f -> k (b i) f", b=2 * CB)
    items_rows = items.rearrange("(Q s q) i -> Q s q i", s=2, q=2)

    ctx = ExitStack()
    with ctx:
        def sb(name, shape, dt=fp32):
            return ctx.enter_context(nc.sbuf_tensor(name, shape, dt))

        def bank(name):
            return ctx.enter_context(nc.psum_tensor(name, [128, BANK], fp32))

        def sem(name):
            return ctx.enter_context(nc.semaphore(name))

        def pair(name, shape, dt=fp32):
            return [sb(f"{name}{i}", shape, dt) for i in range(2)]

        ident = sb("ident", [128, 128])
        w_in_sb = sb("w_in_sb", [128, H])
        w_out_sb = sb("w_out_sb", [128, H])
        w_ih_sb = sb("w_ih_sb", [128, G, 2 * H])
        w_hh_sb = sb("w_hh_sb", [128, G, H])
        b_sb = sb("b_sb", [128, 4])
        bg_sb = sb("bg_sb", [128, 2, G])
        w_ihT = sb("w_ihT", [128, 2, G * H])
        b_rows = sb("b_rows", [128, 2, 128])
        hi_rows = sb("hi_rows", [128, 1])
        lo_rows = sb("lo_rows", [128, 1])
        C_hi = sb("C_hi", [128, 3, G * H], fp32r)
        C_lo = sb("C_lo", [128, 3, G * H], fp32r)
        v_hi = sb("v_hi", [128, G * H], fp32r)
        v_lo = sb("v_lo", [128, G * H])
        v_mask = sb("v_mask", [128, G * H])
        v_rows = sb("v_rows", [128, G * H], fp32r)
        warm = sb("warm", [128, 1])
        gate_bias = sb("gate_bias", [128, G])
        items_sb = sb("items_sb", [128, 2, 2, N], i32)
        items_f = sb("items_f", [128, 2, 2, HALF])
        items_neg = sb("items_neg", [128, 2, 2, HALF])
        idx_all = sb("idx_all", [128, B // 2 + CTILES], u32)

        idx = pair("idx", [128, CTILES], u32)
        A_nat = pair("A_nat", [128, 2, CTILES, HALF])
        rs = pair("rs", [128, 2, CTILES])
        h_nat = pair("h_nat", [128, CTILES, H])
        A_bd = sb("A_bd", [128, 2, 2, 2, P2])
        rs_bd = pair("rs_bd", [128, 2, 2, P2], fp32r)
        hT = pair("hT", [128, CT])
        hT_hi = pair("hT_hi", [128, CT], fp32r)
        hT_lo = pair("hT_lo", [128, CT], fp32r)
        u_hi = pair("u_hi", [128, 2, CT], fp32r)
        u_lo = pair("u_lo", [128, 2, CT], fp32r)
        r_sb = pair("r_sb", [128, CT])
        z_sb = pair("z_sb", [128, CT])
        n_sb = pair("n_sb", [128, CT])
        t_sb = pair("t_sb", [128, CT])
        p_sb = pair("p_sb", [128, CT])
        d_sb = pair("d_sb", [128, CT])
        e_sb = pair("e_sb", [128, CT])
        o_sb = sb("o_sb", [128, 2 * CT])
        out_sb = [sb(f"out_sb{i}", [128, FULL[i], H]) for i in range(2)]
        out_rest = sb("out_rest", [REST, H])

        ps_x = bank("ps_x")
        ps_h = bank("ps_h")
        ps_u = ctx.enter_context(nc.psum_tensor("ps_u", [128, 2, BANK], fp32))
        ps_r = bank("ps_r")
        ps_z = bank("ps_z")
        ps_in = bank("ps_in")
        ps_hn = bank("ps_hn")

        warm_zeroed = sem("warm_zeroed")
        items_zeroed = sem("items_zeroed")
        A_zeroed = sem("A_zeroed")
        rows_zeroed = sem("rows_zeroed")
        h_zeroed = sem("h_zeroed")
        bd_zeroed = sem("bd_zeroed")
        ident_made = sem("ident_made")
        weights_in = sem("weights_in")
        biases_in = sem("biases_in")
        items_in = sem("items_in")
        items_step = sem("items_step")
        items_transposed = sem("items_transposed")
        idx_made = sem("idx_made")
        weights_transposed = sem("weights_transposed")
        w_ihT_copied = sem("w_ihT_copied")
        C_done = sem("C_done")
        C_split = sem("C_split")
        constants_done = sem("constants_done")
        v_hi_made = sem("v_hi_made")
        C_hi_made = sem("C_hi_made")
        lo_rows_step = sem("lo_rows_step")
        b_rows_made = sem("b_rows_made")
        v_step = sem("v_step")
        setup_done = sem("setup_done")

        A_loaded = [sem(f"A_loaded{i}") for i in range(2)]
        h_loaded = [sem(f"h_loaded{i}") for i in range(2)]
        out_stored = [sem(f"out_stored{i}") for i in range(2)]
        rest_stored = sem("rest_stored")
        idx_staged = sem("idx_staged")
        rs_summed = sem("rs_summed")
        rs_hi_put = sem("rs_hi_put")
        rs_put = sem("rs_put")
        AT_done = sem("AT_done")
        hT_done = sem("hT_done")
        agg_done = sem("agg_done")
        hn_done = sem("hn_done")
        r_done = sem("r_done")
        z_done = sem("z_done")
        in_done = sem("in_done")
        outT_done = sem("outT_done")
        A_placed = sem("A_placed")
        hT_copied = sem("hT_copied")
        hT_hi_made = sem("hT_hi_made")
        hT_lo_made = sem("hT_lo_made")
        u_hi_made = sem("u_hi_made")
        u_lo_made = sem("u_lo_made")
        r_made = sem("r_made")
        z_made = sem("z_made")
        n_made = sem("n_made")
        t_made = sem("t_made")
        p_made = sem("p_made")
        d_made = sem("d_made")
        e_made = sem("e_made")
        o_made = sem("o_made")
        out_copied = sem("out_copied")

        def chunks(eng, step, peeled=1):
            for c in range(2 * peeled):
                step(c, c // 2, c % 2)
            with eng.Fori(peeled, NCH // 2 - 1) as k:
                for par in range(2):
                    step(2 * k + par, k, par)
            for par in range(2):
                step(NCH - 2 + par, NCH // 2 - 1, par)

        def number(c):
            return isinstance(c, int)

        block = ctx.enter_context(nc.Block())

        @block.sync
        def _(sp):
            sp.dma_start(items_sb[:, :, :, :], items_rows).then_inc(items_in, 16)

            def load_A(c, par):
                for d in range(2):
                    sp.dma_start(A_nat[par][0:P2, d, :, 0:N],
                                 A_rows[d, bass.ds(c, 1), :, :, :].rearrange("c p g j -> (c p) g j"))\
                      .then_inc(A_loaded[par], 16)

            def load_column(at, b):
                with nc.allow_non_contiguous_dma(reason="a bias, once, a feature on each partition"):
                    sp.dma_start(at, b.rearrange("(g p) -> p g", p=128)).then_inc(biases_in, 16)

            load_column(b_sb[:, 0:1], b_in)
            load_column(b_sb[:, 1:2], b_out)
            load_A(0, 0)
            load_column(b_sb[:, 2:3], b_iah)
            load_column(b_sb[:, 3:4], b_oah)
            load_A(1, 1)
            load_column(bg_sb[:, 0, :], b_ih)
            load_column(bg_sb[:, 1, :], b_hh)

            def store(c, k, par):
                sp.wait_ge(out_copied, c + 1)
                pair_out = out_pairs[bass.ds(k, 1), :, :]
                part = pair_out[:, FROM[par]:FROM[par] + FULL[par] * 128, :]
                sp.dma_start(part.rearrange("k (p t) f -> (k p) t f", t=FULL[par]), out_sb[par][:, :, :])\
                  .then_inc(out_stored[par], 16)
                if par:
                    sp.dma_start(pair_out[:, REST_AT:2 * CT, :].rearrange("k p f -> (k p) f"), out_rest[:, :])\
                      .then_inc(rest_stored, 16)

            def step(c, k, par):
                if not (number(c) and c + 2 >= NCH):
                    sp.wait_ge(AT_done, c + 1)
                    load_A(c + 2, par)
                if not (number(c) and c < 2):
                    store(c - 2, k - 1, par)

            chunks(sp, step)
            for par in range(2):
                store(NCH - 2 + par, NCH // 2 - 1, par)
            for par in range(2):
                sp.wait_ge(out_stored[par], 16 * (NCH // 2))
            sp.wait_ge(rest_stored, 16 * (NCH // 2))

        @block.gpsimd
        def _(pool):
            pool.memset(ident[:, :], 0.0).then_inc(ident_made, 1)
            pool.wait_ge(ident_made, 1)
            pool.affine_select(out=ident[:, :], in_=ident[:, :], compare_op=ALU.not_equal, fill=1.0,
                               base=0, pattern=[[-1, 128]], channel_multiplier=1).then_inc(ident_made, 1)
            for t in h_nat:
                last = pool.memset(t[:], 0.0)
            last.then_inc(h_zeroed, 1)
            pool.memset(lo_rows[:, :], 0.0).then_inc(lo_rows_step, 1)
            for n, row in enumerate([s * HALF + N + d * RS + 1 for s in range(2) for d in range(2)]):
                pool.wait_ge(lo_rows_step, n + 1)
                pool.affine_select(out=lo_rows[:, :], in_=lo_rows[:, :], compare_op=ALU.not_equal, fill=1.0,
                                   base=-row, pattern=[[0, 1]], channel_multiplier=1).then_inc(lo_rows_step, 1)
            pool.wait_ge(idx_made, 1)

            def stage_indices(c, par):
                pool.tensor_copy(idx[par][:, :], idx_all[:, bass.ds(c * CTILES, CTILES)]).then_inc(idx_staged, 1)

            def gather(par):
                for t in range(CTILES):
                    pool.indirect_dma_start(
                        out=h_nat[par][:, t, :], out_offset=None, in_=emb,
                        in_offset=bass.IndirectOffsetOnAxis(ap=idx[par][:, t:t + 1], axis=0),
                        bounds_check=V - 1, oob_is_err=False).then_inc(h_loaded[par], 16)

            stage_indices(0, 0)
            stage_indices(1, 1)
            pool.wait_ge(idx_staged, 2)
            pool.wait_ge(h_zeroed, 1)
            gather(0)
            gather(1)
            pool.wait_ge(h_loaded[0], 16 * CTILES)
            stage_indices(2, 0)

            def step(c, k, par):
                if not (number(c) and c + 2 >= NCH):
                    pool.wait_ge(agg_done, c + 1)
                    pool.wait_ge(idx_staged, c + 3)
                    if not (number(c) and c + 3 >= NCH):
                        pool.wait_ge(h_loaded[1 - par], 16 * CTILES * (k + par + 1))
                        stage_indices(c + 3, 1 - par)
                    gather(par)

            chunks(pool, step)

        @block.scalar
        def _(act):
            act.dma_start(w_ih_sb[:, :, :], w_ih.rearrange("(g p) k -> p g k", p=128)).then_inc(weights_in, 16)
            act.dma_start(w_in_sb[:, :], w_in).then_inc(weights_in, 16)
            act.dma_start(w_out_sb[:, :], w_out).then_inc(weights_in, 16)
            act.dma_start(w_hh_sb[:, :, :], w_hh.rearrange("(g p) k -> p g k", p=128)).then_inc(weights_in, 16)
            act.wait_ge(warm_zeroed, 1)
            act.activation(warm[:, :], warm[:, :], ACT.Sigmoid)
            act.wait_ge(weights_transposed, 1)
            act.activation(w_ihT[:, 0, :], ps_r[:, 0:G * H], ACT.Copy)
            act.activation(w_ihT[:, 1, :], ps_z[:, 0:G * H], ACT.Copy).then_inc(w_ihT_copied, 1)
            act.activation(C_hi[:, 2, :], ps_hn[:, 0:G * H], ACT.Copy).then_inc(C_hi_made, 1)
            def place_A(c, par):
                act.wait_ge(AT_done, c + 1)
                if not (number(c) and c < 1):
                    act.wait_ge(agg_done, c)
                if not (number(c) and c < 2):
                    act.wait_ge(z_done, c - 1)
                x = ps_x[:, 0:2 * 2 * P2].rearrange("p (Q d t) -> p Q d t", Q=2, d=2)
                for s in range(2):
                    lo = s * HALF
                    act.activation(A_bd[lo:lo + HALF, :, s, :, :], x[lo:lo + HALF, :, :, :], ACT.Copy)
                    last = act.activation(rs_bd[par][lo + 32:lo + HALF, :, s, :], x[lo + 32:lo + HALF, :, 0, :], ACT.Copy)
                last.then_inc(A_placed, 1)

            def copy_h(c, par):
                act.wait_ge(hT_done, c + 1)
                if not (number(c) and c < 2):
                    act.wait_ge(d_made, c - 1)
                src = ps_h[:, :].rearrange("p (Q q s i) -> p Q q s i", Q=2, q=2, s=2)
                dst = hT[par][:, :].rearrange("p (Q s q i) -> p Q q s i", Q=2, s=2, q=2)
                for Q in range(2):
                    last = act.activation(dst[:, Q], src[:, Q, :, :, 0:N], ACT.Copy)
                last.then_inc(hT_copied, 1)

            def split_u(c, par):
                act.wait_ge(agg_done, c + 1)
                if not (number(c) and c < 2):
                    act.wait_ge(z_done, c - 1)
                src = ps_u[:, :, 0:CT].rearrange("p Q (d t) -> p Q d t", d=2)
                dst = u_hi[par][:, :, :].rearrange("p d (Q t) -> p Q d t", Q=2)
                act.activation(dst, src, ACT.Copy).then_inc(u_hi_made, 1)

            def copy_out(c, k, par):
                act.wait_ge(outT_done, c + 1)
                if not (number(k) and k < 1):
                    act.wait_ge(out_stored[par], 16 * k)
                    if par:
                        act.wait_ge(rest_stored, 16 * k)
                n = FULL[par] * H
                last = act.activation(out_sb[par][:, :, :], ps_x[:, 0:n].rearrange("p (t f) -> p t f", f=H), ACT.Copy)
                if par:
                    last = act.activation(out_rest[:, :], ps_x[0:REST, n:n + H], ACT.Copy)
                last.then_inc(out_copied, 1)

            act.wait_ge(bd_zeroed, 1)
            place_A(0, 0)
            act.wait_ge(C_done, 1)
            act.activation(C_hi[:, 0, :], ps_r[:, 0:G * H], ACT.Copy)
            act.activation(C_hi[:, 1, :], ps_z[:, 0:G * H], ACT.Copy).then_inc(C_hi_made, 1)
            copy_h(0, 0)
            split_u(0, 0)
            act.wait_ge(constants_done, 1)
            act.activation(v_hi[:, :], ps_in[:, 0:G * H], ACT.Copy).then_inc(v_hi_made, 1)
            act.wait_ge(setup_done, 1)

            def step(c, k, par):
                if not (number(c) and c + 1 >= NCH):
                    place_A(c + 1, 1 - par)
                    copy_h(c + 1, 1 - par)
                act.wait_ge(r_done, c + 1)
                if not (number(c) and c < 2):
                    act.wait_ge(t_made, c - 1)
                act.activation(r_sb[par][:, :], ps_r[:, 0:CT], ACT.Sigmoid, bias=gate_bias[:, 0:1]).then_inc(r_made, 1)
                if not (number(c) and c + 1 >= NCH):
                    split_u(c + 1, 1 - par)
                if not (number(c) and c < 1):
                    copy_out(c - 1, k if par else k - 1, 1 - par)
                act.wait_ge(p_made, c + 1)
                if not (number(c) and c < 2):
                    act.wait_ge(o_made, c - 1)
                act.activation(n_sb[par][:, :], p_sb[par][:, :], ACT.Tanh, bias=gate_bias[:, 2:3]).then_inc(n_made, 1)
                act.wait_ge(z_done, c + 1)
                if not (number(c) and c < 2):
                    act.wait_ge(e_made, c - 1)
                act.activation(z_sb[par][:, :], ps_z[:, 0:CT], ACT.Sigmoid, bias=gate_bias[:, 1:2]).then_inc(z_made, 1)

            chunks(act, step, peeled=2)
            copy_out(NCH - 1, NCH // 2 - 1, 1)

        @block.vector
        def _(dve):
            dve.memset(warm[:, :], 0.0).then_inc(warm_zeroed, 1)
            dve.memset(items_f[:], SKIP).then_inc(items_zeroed, 1)
            for t in A_nat:
                last = dve.memset(t[:, :, :, N:HALF], 0.0)
            last.then_inc(A_zeroed, 1)
            dve.memset(idx_all[:, B // 2:B // 2 + CTILES], 0)
            dve.memset(b_rows[:], 0.0).then_inc(rows_zeroed, 1)

            dve.wait_ge(items_zeroed, 1)
            dve.wait_ge(items_in, 16)
            body = items_f[:, :, :, 0:N]
            neg = items_neg[:, :, :, 0:N]
            given = items_sb[:, :, :, :].rearrange("p s q i -> p q s i")
            dve.tensor_scalar(neg, given, 0.0, float(V), ALU.is_lt, ALU.mult).then_inc(items_step, 1)
            dve.wait_ge(items_step, 1)
            dve.tensor_tensor(body, given, neg, ALU.add).then_inc(items_step, 1)
            dve.wait_ge(items_step, 2)
            dve.tensor_scalar(body, body, 0.0, float(V - 1), ALU.max, ALU.min).then_inc(items_step, 1)
            dve.wait_ge(items_transposed, 1)
            dve.tensor_copy(idx_all[:, 0:B // 2].rearrange("p (Q q) -> p q Q", q=2),
                            ps_h[:, 0:B // 2].rearrange("p (q Q) -> p q Q", q=2)).then_inc(idx_made, 1)

            def put_row_sums(c, k, par):
                dve.wait_ge(A_loaded[par], 32 * (k + 1))
                dve.tensor_reduce(out=rs[par][0:P2, :, :],
                                  in_=A_nat[par][0:P2, :, :, 0:N],
                                  axis=AX.X, op=ALU.add).then_inc(rs_summed, 1)
                dve.wait_ge(rs_summed, c + 1)
                slots = A_nat[par][0:P2, 0, :, N:N + 2 * RS].rearrange("p g (d x) -> p d g x", d=2)
                dve.tensor_copy(slots[:, :, :, 0:2].bitcast(fp32r),
                                rs[par][0:P2, :, :].unsqueeze(3).to_broadcast([P2, 2, CTILES, 2]))\
                   .then_inc(rs_hi_put, 1)
                dve.wait_ge(rs_hi_put, c + 1)
                dve.tensor_tensor(slots[:, :, :, 2], rs[par][0:P2, :, :], slots[:, :, :, 0], ALU.subtract)\
                   .then_inc(rs_put, 1)

            dve.wait_ge(A_zeroed, 1)
            put_row_sums(0, 0, 0)

            dve.memset(A_bd[:], 0.0)
            for t in rs_bd:
                last = dve.memset(t[:].bitcast(fp32), 0.0)
            last.then_inc(bd_zeroed, 1)

            dve.wait_ge(rows_zeroed, 1)
            dve.wait_ge(biases_in, 96)
            for half in range(2):
                for d in range(2):
                    at = half * HALF + N + d * RS
                    last = dve.tensor_copy(b_rows[:, d, at:at + RS], b_sb[:, d:d + 1].to_broadcast([128, RS]))
            last.then_inc(b_rows_made, 1)
            dve.wait_ge(C_hi_made, 1)
            dve.tensor_tensor(C_lo[:, 2, :], ps_hn[:, 0:G * H], C_hi[:, 2, :].bitcast(fp32), ALU.subtract)
            dve.wait_ge(C_hi_made, 2)
            for d, ps in enumerate((ps_r, ps_z)):
                last = dve.tensor_tensor(C_lo[:, d, :], ps[:, 0:G * H], C_hi[:, d, :].bitcast(fp32), ALU.subtract)
            last.then_inc(C_split, 1)
            put_row_sums(1, 0, 1)

            def split_h(c, par):
                dve.wait_ge(hT_copied, c + 1)
                if not (number(c) and c < 2):
                    dve.wait_ge(z_done, c - 1)
                dve.tensor_copy(hT_hi[par][:, :], hT[par][:, :]).then_inc(hT_hi_made, 1)
                dve.wait_ge(hT_hi_made, c + 1)
                dve.tensor_tensor(hT_lo[par][:, :], hT[par][:, :], hT_hi[par][:, :].bitcast(fp32), ALU.subtract)\
                   .then_inc(hT_lo_made, 1)

            def split_u(c, par):
                dve.wait_ge(u_hi_made, c + 1)
                src = ps_u[:, :, 0:CT].rearrange("p Q (d t) -> p Q d t", d=2)
                hi = u_hi[par][:, :, :].rearrange("p d (Q t) -> p Q d t", Q=2).bitcast(fp32)
                dst = u_lo[par][:, :, :].rearrange("p d (Q t) -> p Q d t", Q=2)
                dve.tensor_tensor(dst, src, hi, ALU.subtract).then_inc(u_lo_made, 1)

            split_h(0, 0)
            split_u(0, 0)
            dve.wait_ge(lo_rows_step, 5)
            dve.tensor_scalar(hi_rows[:, :], lo_rows[:, :], -1.0, 1.0, ALU.mult, ALU.add).then_inc(v_step, 1)
            dve.wait_ge(v_hi_made, 1)
            dve.tensor_tensor(v_lo[:, :], ps_in[:, 0:G * H], v_hi[:, :].bitcast(fp32), ALU.subtract).then_inc(v_step, 1)
            dve.wait_ge(v_step, 2)
            dve.tensor_scalar(v_mask[:, :], v_lo[:, :], lo_rows[:, 0:1], None, ALU.mult).then_inc(v_step, 1)
            dve.wait_ge(v_step, 3)
            dve.scalar_tensor_tensor(out=v_rows[:, :], in0=v_hi[:, :].bitcast(fp32), scalar=hi_rows[:, 0:1],
                                     in1=v_mask[:, :], op0=ALU.mult, op1=ALU.add)
            dve.tensor_tensor(gate_bias[:, :], ps_in[:, BANK - G:BANK], bg_sb[:, 0, :], ALU.add).then_inc(v_step, 1)
            dve.wait_ge(v_step, 4)
            dve.tensor_tensor(gate_bias[:, 0:2], gate_bias[:, 0:2], bg_sb[:, 1, 0:2], ALU.add).then_inc(setup_done, 1)

            def step(c, k, par):
                if not (number(c) and c + 1 >= NCH):
                    split_h(c + 1, 1 - par)
                dve.wait_ge(r_made, c + 1)
                dve.wait_ge(hn_done, c + 1)
                dve.scalar_tensor_tensor(out=t_sb[par][:, :], in0=ps_hn[:, 0:CT], scalar=bg_sb[:, 1, 2:3],
                                         in1=r_sb[par][:, :], op0=ALU.add, op1=ALU.mult).then_inc(t_made, 1)
                if not (number(c) and c + 2 >= NCH):
                    put_row_sums(c + 2, k + 1, par)
                if not (number(c) and c + 1 >= NCH):
                    split_u(c + 1, 1 - par)
                dve.wait_ge(in_done, c + 1)
                dve.wait_ge(t_made, c + 1)
                dve.tensor_tensor(p_sb[par][:, :], ps_in[:, 0:CT], t_sb[par][:, :], ALU.add).then_inc(p_made, 1)
                dve.wait_ge(n_made, c + 1)
                dve.tensor_tensor(d_sb[par][:, :], hT[par][:, :], n_sb[par][:, :], ALU.subtract).then_inc(d_made, 1)
                dve.wait_ge(d_made, c + 1)
                dve.wait_ge(z_made, c + 1)
                dve.tensor_tensor(e_sb[par][:, :], d_sb[par][:, :], z_sb[par][:, :], ALU.mult).then_inc(e_made, 1)
                dve.wait_ge(e_made, c + 1)
                if not (number(c) and c < 2):
                    dve.wait_ge(outT_done, c - par)
                dve.tensor_tensor(o_sb[:, par * CT:par * CT + CT], e_sb[par][:, :], n_sb[par][:, :], ALU.add)\
                   .then_inc(o_made, 1)

            chunks(dve, step)

        @block.tensor
        def _(pe):
            pe.wait_ge(ident_made, 2)
            pe.wait_ge(items_step, 3)
            for q in range(2):
                last = pe.transpose(ps_h[:, q * 128:q * 128 + 128],
                                    items_f[:, q, :, :].rearrange("p s i -> p (s i)"), ident[:, :])
            last.then_inc(items_transposed, 1)
            pe.wait_ge(weights_in, 64)
            for g in range(G):
                at = slice(g * H, g * H + H)
                pe.transpose(ps_r[:, at], w_ih_sb[:, g, 0:H], ident[:, :])
                pe.transpose(ps_z[:, at], w_ih_sb[:, g, H:2 * H], ident[:, :])
                last = pe.transpose(ps_hn[:, at], w_hh_sb[:, g, :], ident[:, :])
            last.then_inc(weights_transposed, 1)

            def row_sum_rows():
                pe.wait_ge(b_rows_made, 1)
                for d in range(2):
                    pe.matmul(ps_in[:, 0:G * H], b_rows[:, d, :], w_ihT[:, d, :], start=d == 0, stop=d == 1)

            def constants():
                for g in range(G):
                    for d in range(2):
                        last = pe.matmul(ps_in[:, BANK - G + g:BANK - G + g + 1], w_ihT[:, d, g * H:g * H + H],
                                         b_sb[:, 2 + d:3 + d], start=d == 0, stop=d == 1)
                last.then_inc(constants_done, 1)

            def transpose_A(c, k, par):
                pe.wait_ge(A_loaded[par], 32 * (k + 1))
                pe.wait_ge(rs_put, c + 1)
                if not (number(c) and c < 3):
                    pe.wait_ge(out_copied, c - 2)
                for Q in range(2):
                    for d in range(2):
                        at = (2 * Q + d) * P2
                        last = pe.transpose(ps_x[:, at:at + P2],
                                            A_nat[par][0:P2, d, 2 * Q:2 * Q + 2, :].rearrange("p s j -> p (s j)"),
                                            ident[0:P2, 0:P2])
                last.then_inc(AT_done, 1)

            def transpose_h(c, k, par):
                pe.wait_ge(h_loaded[par], 16 * CTILES * (k + 1))
                if not (number(c) and c < 1):
                    pe.wait_ge(hT_copied, c)
                else:
                    pe.wait_ge(idx_made, 1)
                for t in range(CTILES):
                    last = pe.transpose(ps_h[:, t * 128:t * 128 + ROWS], h_nat[par][0:ROWS, t, :],
                                        ident[0:ROWS, 0:ROWS])
                last.then_inc(hT_done, 1)

            def aggregate(c, par):
                pe.wait_ge(A_placed, c + 1)
                if not (number(c) and c < 1):
                    pe.wait_ge(u_lo_made, c)
                for Q in range(2):
                    u = ps_u[:, Q, 0:CT].rearrange("p (d s q i) -> p s d q i", d=2, s=2, q=2)
                    for q in range(2):
                        last = pe.matmul(u[:, :, :, q, :], h_nat[par][:, 2 * Q + q, :],
                                         A_bd[:, Q, :, :, q * N:q * N + N], start=True, stop=True)
                last.then_inc(agg_done, 1)

            def gate(psum, g, par, terms):
                at = slice(g * H, g * H + H)
                products = []
                for w, hi, lo in terms:
                    products += [(C_hi[:, w, at], hi), (C_lo[:, w, at], hi), (C_hi[:, w, at], lo)]
                if terms[0][0] == 0:
                    products.append((v_rows[:, at], rs_bd[par][:, :, :, :].rearrange("p Q s t -> p (Q s t)")))
                for n, (w, x) in enumerate(products):
                    last = pe.matmul(psum[:, 0:CT], w, x, start=n == 0, stop=n == len(products) - 1)
                return last

            transpose_A(0, 0, 0)
            pe.wait_ge(w_ihT_copied, 1)
            pe.matmul(ps_r[:, 0:G * H], w_in_sb[:, :], w_ihT[:, 0, :], start=True, stop=True)
            pe.matmul(ps_z[:, 0:G * H], w_out_sb[:, :], w_ihT[:, 1, :], start=True, stop=True).then_inc(C_done, 1)
            row_sum_rows()
            transpose_h(0, 0, 0)
            aggregate(0, 0)
            constants()
            pe.wait_ge(C_split, 1)

            def step(c, k, par):
                of_u = [(d, u_hi[par][:, d, :], u_lo[par][:, d, :]) for d in range(2)]
                of_h = [(2, hT_hi[par][:, :], hT_lo[par][:, :])]
                more = not (number(c) and c + 1 >= NCH)
                if more:
                    transpose_A(c + 1, k + par, 1 - par)
                    transpose_h(c + 1, k + par, 1 - par)
                pe.wait_ge(hT_lo_made, c + 1)
                if not (number(c) and c < 1):
                    pe.wait_ge(t_made, c)
                gate(ps_hn, 2, par, of_h).then_inc(hn_done, 1)
                if number(c) and c < 1:
                    pe.wait_ge(setup_done, 1)
                pe.wait_ge(u_lo_made, c + 1)
                if not (number(c) and c < 1):
                    pe.wait_ge(r_made, c)
                gate(ps_r, 0, par, of_u + of_h).then_inc(r_done, 1)
                if more:
                    aggregate(c + 1, 1 - par)
                if not (number(c) and c < 1):
                    transpose_out(c - 1, 1 - par, more)
                if not (number(c) and c < 1):
                    pe.wait_ge(p_made, c)
                gate(ps_in, 2, par, of_u).then_inc(in_done, 1)
                if not (number(c) and c < 1):
                    pe.wait_ge(z_made, c)
                gate(ps_z, 1, par, of_u + of_h).then_inc(z_done, 1)

            def transpose_out(c, par, more):
                pe.wait_ge(o_made, c + 1)
                if more:
                    pe.wait_ge(A_placed, c + 3)
                else:
                    pe.wait_ge(out_copied, c)
                for t in range(FULL[par]):
                    at = FROM[par] + t
                    last = pe.transpose(ps_x[:, t * H:t * H + H],
                                        o_sb[:, at:FROM[par] + FULL[par] * 128:FULL[par]], ident[:, :])
                if par:
                    last = pe.transpose(ps_x[0:REST, FULL[par] * H:FULL[par] * H + H], o_sb[:, REST_AT:2 * CT],
                                        ident[:, :])
                last.then_inc(outT_done, 1)

            chunks(pe, step)
            transpose_out(NCH - 1, 1, False)


_INS = ['r_A', 'r_items', 'L0_rec_emb', 'L0_rec_w_in', 'L0_rec_b_in', 'L0_rec_w_out', 'L0_rec_b_out',
        'L0_rec_w_ih', 'L0_rec_w_hh', 'L0_rec_b_ih', 'L0_rec_b_hh', 'L0_rec_b_iah', 'L0_rec_b_oah']


def kernel(**inputs):
    import numpy as _np
    import concourse.bacc as _bacc
    from concourse import mybir as _mybir
    from concourse.bass_utils import run_bass_kernel_spmd as _run

    nc = _bacc.Bacc("TRN2", target_bir_lowering=False, num_devices=1)
    arrays, args = {}, []
    for name in _INS:
        a = _np.ascontiguousarray(inputs[name])
        arrays[f"in_{name}_dram"] = a
        args.append(nc.dram_tensor(f"in_{name}_dram", a.shape, _mybir.dt.from_np(a.dtype), kind="ExternalInput").ap())
    B, N = arrays["in_r_items_dram"].shape
    H = arrays["in_L0_rec_emb_dram"].shape[1]
    args.append(nc.dram_tensor("out_0_dram", (B, N, H), _mybir.dt.float32, kind="ExternalOutput").ap())
    gnn_cell_kernel(nc, *args)
    r = _run(nc, [arrays], core_ids=[0])
    return r.results[0]["out_0_dram"]
```
